# Optimizing a Trainium2 kernel written in Bass

```python
import numpy as np
import jax
import jax.numpy as jnp

def _softmax(x, axis=-1):
    return jax.nn.softmax(x, axis=axis)

def _gelu(x):
    return jax.nn.gelu(x, approximate=True)

def _silu(x):
    return jax.nn.silu(x)

def _sigmoid(x):
    return jax.nn.sigmoid(x)

def _layernorm(x, axis=-1, eps=1e-05):
    m = jnp.mean(x, axis=axis, keepdims=True)
    v = jnp.var(x, axis=axis, keepdims=True)
    return (x - m) / jnp.sqrt(v + eps)

def _scatter_add(tgt, idx, src, axis=0):
    return tgt.at[idx].add(src)

def _segment_sum(src, seg, n):
    return jax.ops.segment_sum(src, seg, n)
kernel_name = 'mk_adaln_ffn_d1_seqx_r4_ce48df'

def setup_inputs(seed: int=0):
    np.random.seed(seed)
    _w = jnp.asarray

    def _rec_inputs():
        import jax
        import jax.numpy as jnp
        _rk = jax.random.key(seed)
        x = -8.015e-05 + 0.9999 * jax.random.normal(jax.random.fold_in(_rk, 1), (64, 64, 512), jnp.float32)
        _lenS = 64 - jax.random.randint(jax.random.fold_in(_rk, 7), (64,), 0, max(1, 64 // 4) + 1, jnp.int32)
        _lenS2 = 64 - jax.random.randint(jax.random.fold_in(_rk, 8), (64,), 0, max(1, 64 // 4) + 1, jnp.int32)
        cond_1024 = 0.00191187 + 0.999416 * jax.random.normal(jax.random.fold_in(_rk, 11), (64, 256), jnp.float32)
        return (x, cond_1024)
    x, cond_1024 = _rec_inputs()

    def _L0_cond_setup():
        import jax, jax.numpy as jnp
        import numpy as np
        B, N, V_DIM, Q_DIM = (64, 100, 512, 256)
        key = jax.random.key(seed)
        k1, k2, k3, k4 = jax.random.split(key, 4)
        v = jax.random.normal(k1, (B, N, V_DIM), dtype=jnp.float32)
        q = jax.random.normal(k2, (B, Q_DIM), dtype=jnp.float32)
        W3 = jax.random.normal(k3, (Q_DIM, V_DIM), dtype=jnp.float32) * (1.0 / np.sqrt(Q_DIM))
        b3 = jnp.zeros((V_DIM,), dtype=jnp.float32)
        W2 = jax.random.normal(k4, (V_DIM, V_DIM), dtype=jnp.float32) * (1.0 / np.sqrt(V_DIM))
        b2 = jnp.zeros((V_DIM,), dtype=jnp.float32)
        return {'v': v, 'q': q, 'W3': W3, 'b3': b3, 'W2': W2, 'b2': b2}
    _L0_cond_all = _L0_cond_setup()
    _L0_cond_in = {k: v for k, v in _L0_cond_all.items() if k in ('W3', 'b3', 'W2', 'b2')}
    del _L0_cond_all

    def _L0_ffn_setup():
        import jax, jax.numpy as jnp
        import numpy as np
        BLOCK = 64

        def dequant4bit(q, scale):
            return (q.astype(jnp.float32) - 7.5) * jnp.repeat(scale, BLOCK, axis=1)
        key = jax.random.key(seed)
        ks = jax.random.split(key, 11)
        B, S, D, H, R = (4, 512, 512, 2048, 16)
        return {'x1': jax.random.normal(ks[0], (B, S, D), jnp.float32), 'w_up_q': jax.random.randint(ks[1], (H, D), 0, 16, dtype=jnp.int32), 'w_up_scale': jax.random.uniform(ks[2], (H, D // BLOCK), jnp.float32) * 0.02, 'b_up': jax.random.normal(ks[3], (H,), jnp.float32) * 0.01, 'w_up_lora_a': jax.random.normal(ks[4], (D, R), jnp.float32) * 0.02, 'w_up_lora_b': jax.random.normal(ks[5], (R, H), jnp.float32) * 0.02, 'w_down_q': jax.random.randint(ks[6], (D, H), 0, 16, dtype=jnp.int32), 'w_down_scale': jax.random.uniform(ks[7], (D, H // BLOCK), jnp.float32) * 0.02, 'b_down': jax.random.normal(ks[8], (D,), jnp.float32) * 0.01, 'w_down_lora_a': jax.random.normal(ks[9], (H, R), jnp.float32) * 0.02, 'w_down_lora_b': jax.random.normal(ks[10], (R, D), jnp.float32) * 0.02}
    _L0_ffn_all = _L0_ffn_setup()
    _L0_ffn_in = {k: v for k, v in _L0_ffn_all.items() if k in ('w_up_q', 'w_up_scale', 'b_up', 'w_up_lora_a', 'w_up_lora_b', 'w_down_q', 'w_down_scale', 'b_down', 'w_down_lora_a', 'w_down_lora_b')}
    del _L0_ffn_all
    return {'x': x, 'cond_1024': cond_1024, 'L0_cond_W3': _L0_cond_in['W3'], 'L0_cond_b3': _L0_cond_in['b3'], 'L0_cond_W2': _L0_cond_in['W2'], 'L0_cond_b2': _L0_cond_in['b2'], 'L0_ffn_w_up_q': _L0_ffn_in['w_up_q'], 'L0_ffn_w_up_scale': _L0_ffn_in['w_up_scale'], 'L0_ffn_b_up': _L0_ffn_in['b_up'], 'L0_ffn_w_up_lora_a': _L0_ffn_in['w_up_lora_a'], 'L0_ffn_w_up_lora_b': _L0_ffn_in['w_up_lora_b'], 'L0_ffn_w_down_q': _L0_ffn_in['w_down_q'], 'L0_ffn_w_down_scale': _L0_ffn_in['w_down_scale'], 'L0_ffn_b_down': _L0_ffn_in['b_down'], 'L0_ffn_w_down_lora_a': _L0_ffn_in['w_down_lora_a'], 'L0_ffn_w_down_lora_b': _L0_ffn_in['w_down_lora_b']}

def reference(x, cond_1024, L0_cond_W3, L0_cond_b3, L0_cond_W2, L0_cond_b2, L0_ffn_w_up_q, L0_ffn_w_up_scale, L0_ffn_b_up, L0_ffn_w_up_lora_a, L0_ffn_w_up_lora_b, L0_ffn_w_down_q, L0_ffn_w_down_scale, L0_ffn_b_down, L0_ffn_w_down_lora_a, L0_ffn_w_down_lora_b):
    import jax
    import jax.numpy as jnp

    def _L0_cond_ref(v, q, W3, b3, W2, b2):
        import jax, jax.numpy as jnp
        import numpy as np
        B, N, V_DIM, Q_DIM = (64, 100, 512, 256)
        q_emb = jax.nn.relu(q @ W3 + b3)
        n = v.shape[1]
        v_sum = jnp.sum(v, axis=1, keepdims=True)
        x = (n * v + v_sum) * q_emb[:, None, :]
        return jax.nn.relu(x @ W2 + b2)

    def _L0_ffn_ref(x1, w_up_q, w_up_scale, b_up, w_up_lora_a, w_up_lora_b, w_down_q, w_down_scale, b_down, w_down_lora_a, w_down_lora_b):
        import jax, jax.numpy as jnp
        import numpy as np
        BLOCK = 64

        def dequant4bit(q, scale):
            return (q.astype(jnp.float32) - 7.5) * jnp.repeat(scale, BLOCK, axis=1)
        w_up = dequant4bit(w_up_q, w_up_scale).T
        y1 = x1 @ w_up + b_up + x1 @ w_up_lora_a @ w_up_lora_b
        x2 = jax.nn.relu(y1)
        w_down = dequant4bit(w_down_q, w_down_scale).T
        y2 = x2 @ w_down + b_down + x2 @ w_down_lora_a @ w_down_lora_b
        return y2
    x = x + _L0_ffn_ref(_L0_cond_ref(x, cond_1024, L0_cond_W3, L0_cond_b3, L0_cond_W2, L0_cond_b2), L0_ffn_w_up_q, L0_ffn_w_up_scale, L0_ffn_b_up, L0_ffn_w_up_lora_a, L0_ffn_w_up_lora_b, L0_ffn_w_down_q, L0_ffn_w_down_scale, L0_ffn_b_down, L0_ffn_w_down_lora_a, L0_ffn_w_down_lora_b)
    return x

_drawn_inputs = setup_inputs


def setup_inputs(seed=0):
    import zlib

    import numpy as np

    out = dict(_drawn_inputs(seed))
    spreads = {'L0_cond_b3': (0.0, 0.1), 'L0_cond_b2': (0.0, 2.0)}
    factors = {'L0_ffn_b_up': 200.0, 'L0_ffn_b_down': 200.0}
    for name, (base, spread) in spreads.items():
        noise = np.random.default_rng([zlib.crc32(name.encode()), seed]).standard_normal(out[name].shape)
        drawn = base * np.exp(spread * noise) if base else spread * noise
        out[name] = jnp.asarray(drawn.astype(out[name].dtype))
    for name, factor in factors.items():
        out[name] = (out[name] * factor).astype(out[name].dtype)
    return out
```

```python
from contextlib import ExitStack

import concourse.bass as bass
from concourse import mybir

P = 128
QUAD = 32
BANK = 512
PARTS = 3
ALU = mybir.AluOpType
ACT = mybir.ActivationFunctionType
AXIS_X = mybir.AxisListType.X
F32 = mybir.dt.float32
F32R = mybir.dt.float32r
I32 = mybir.dt.int32


def adaln_ffn(nc, x, cond, w3, w2, biases, q_up, q_down, narrow, records, out):
    BLOCKS, _, KD, ROWS = x.shape
    KC, BATCH = cond.shape[1], cond.shape[2]
    D = KD * P
    NH = q_up.shape[1]
    SEQ = 64
    PER_BLOCK = ROWS // SEQ
    ZERO_POINT = 7.5
    X2_SLOTS, XM_SLOTS, FULL_SLOTS = 3, 2, 2
    LAG = 2
    HELD = NH - LAG
    EVACS = NH + KD
    CHUNKS = 2 * NH
    Q_GROUPS = [(0, 1), (1, 2), (2, 4), (4, 8), (8, NH)]
    REC_FIRST = 2
    assert ROWS == BANK and BLOCKS >= 3 and KD == 4

    with ExitStack() as ctx:
        base = (nc.sbuf_base + 63) // 64 * 64
        size = {}
        place = {}
        at = base
        for name, count in [
            ("w_up_hi", NH * D), ("w_up_lo", NH * D), ("w_down_hi", NH * D), ("w_down_lo", NH * D),
            ("w2_hi", KD * D), ("w2_lo", KD * D), ("x_in", KD * ROWS), ("res", KD * ROWS),
            ("xm_hi", XM_SLOTS * ROWS), ("xm_lo", XM_SLOTS * ROWS), ("x1_hi", KD * ROWS), ("x1_lo", KD * ROWS),
            ("x2_hi", X2_SLOTS * ROWS), ("x2_lo", X2_SLOTS * ROWS), ("full", FULL_SLOTS * ROWS),
            ("gate", KD * BATCH), ("sums", KD * PER_BLOCK), ("biases", biases.shape[1]), ("narrow", 3 * D),
        ]:
            place[name] = at
            at += (4 * count + 31) // 32 * 32
        ctx.enter_context(nc.sbuf_tensor("arena", [P, (at - nc.sbuf_base + 3) // 4 + 8], F32))

        def sb(name, shape, dt, over=None, skip=0):
            return nc.alloc_sbuf_tensor_at(name, shape, dt, offset=place[over or name] + skip)

        w_up_hi = sb("w_up_hi", [P, NH, KD, P], F32R)
        w_up_lo = sb("w_up_lo", [P, NH, KD, P], F32R)
        w_down_hi = sb("w_down_hi", [P, NH, D], F32R)
        w_down_lo = sb("w_down_lo", [P, NH, D], F32R)
        w2_hi = sb("w2_hi", [P, KD, D], F32R)
        w2_lo = sb("w2_lo", [P, KD, D], F32R)
        x_in = sb("x_in", [P, KD, ROWS], F32)
        res = sb("res", [P, KD, ROWS], F32)
        xm_hi = sb("xm_hi", [P, XM_SLOTS, ROWS], F32R)
        xm_lo = sb("xm_lo", [P, XM_SLOTS, ROWS], F32R)
        x1_hi = sb("x1_hi", [P, KD, ROWS], F32R)
        x1_lo = sb("x1_lo", [P, KD, ROWS], F32R)
        x2_hi = sb("x2_hi", [P, X2_SLOTS, ROWS], F32R)
        x2_lo = sb("x2_lo", [P, X2_SLOTS, ROWS], F32R)
        full = sb("full", [P, FULL_SLOTS, ROWS], F32)
        gate = sb("gate", [P, KD, BATCH], F32)
        sums = sb("sums", [P, KD, PER_BLOCK], F32)
        bias = sb("biases", [P, biases.shape[1]], F32)
        b_up, b_down = bias[:, 0:NH], bias[:, NH:NH + KD]
        b2, b3 = bias[:, NH + KD:NH + 2 * KD], bias[:, NH + 2 * KD:NH + 3 * KD]
        narrow_r = sb("narrow", [P, 3, D], F32R)
        scale_down, lora_up, lora_down = narrow_r[:, 0, :], narrow_r[:, 1, :], narrow_r[:, 2, :]
        codes_up = sb("codes_up", [P, NH, D], I32, over="w_up_lo")
        codes_down = sb("codes_down", [P, NH, D], I32, over="w_down_lo")
        REC = 3 * P
        REC_SKIP = 4 * NH * (D - REC)
        raw_narrow = sb("raw_narrow", [P, 4, D], F32, over="w_up_hi")
        raw_records = sb("raw_records", [P, NH, REC], F32, over="w_up_hi", skip=REC_SKIP)
        record = sb("record", [P, NH, REC], F32R, over="w_down_hi", skip=REC_SKIP)
        raw_w2 = sb("raw_w2", [P, KD, D], F32, over="w_down_hi")
        assert 4 * 4 * D <= REC_SKIP
        weight = sb("weight", [P, 2, D], F32, over="res")
        expand_up = sb("expand_up", [P, D], F32R, over="res", skip=2 * 4 * D)
        raw_w3 = sb("raw_w3", [P, KC, D], F32, over="x2_hi")
        raw_cond = sb("raw_cond", [P, KC, BATCH], F32, over="x2_lo")

        acc = [ctx.enter_context(nc.psum_tensor(f"acc{m}", [P, BANK], F32)) for m in range(KD)]
        up_ps = [ctx.enter_context(nc.psum_tensor(f"up_ps{m}", [P, BANK], F32)) for m in range(2)]
        scale_ps = ctx.enter_context(nc.psum_tensor("scale_ps", [P, BANK], F32))
        lora_ps = ctx.enter_context(nc.psum_tensor("lora_ps", [P, BANK], F32))
        w2_ps = [up_ps[0], up_ps[1], scale_ps, lora_ps]

        def sem(name):
            return ctx.enter_context(nc.semaphore(name))

        cond_loaded, bias_loaded, narrow_loaded = sem("cond_loaded"), sem("bias_loaded"), sem("narrow_loaded")
        w2_loaded = [sem(f"w2_loaded{k}") for k in range(KD)]
        record_loaded = [sem(f"record_loaded{g}") for g in range(2)]
        codes_loaded = [sem(f"codes_loaded{g}") for g in range(len(Q_GROUPS))]
        x_loaded = [sem(f"x_loaded{k}") for k in range(KD)]
        res_loaded, out_stored = sem("res_loaded"), sem("out_stored")
        w2_cast, w2_split = sem("w2_cast"), sem("w2_split")
        narrow_cast, narrow_split = sem("narrow_cast"), sem("narrow_split")
        record_cast, record_split = sem("record_cast"), sem("record_split")
        gate_ready, gate_done = sem("gate_ready"), sem("gate_done")
        scale_ready, lora_ready = sem("scale_ready"), sem("lora_ready")
        dequant_done, weight_full, weight_hi, weight_ready = (
            sem("dequant_done"), sem("weight_full"), sem("weight_hi"), sem("weight_ready"))
        summed, shifted, modulated = sem("summed"), sem("shifted"), sem("modulated")
        xm_hi_done, xm_split = sem("xm_hi_done"), sem("xm_split")
        w2_step_done = sem("w2_step_done")
        product_ready, relu_done, act_hi_done, act_split = (
            sem("product_ready"), sem("relu_done"), sem("act_hi_done"), sem("act_split"))
        down_done = sem("down_done")
        acc_done, out_ready = sem("acc_done"), sem("out_ready")

        def before(block):
            return KD + EVACS * block

        block = ctx.enter_context(nc.Block())

        @block.sync
        def _(sp):
            def load_x(b):
                for k in range(KD):
                    sp.dma_start(x_in[:, k, :], x[b, :, k, :]).then_inc(x_loaded[k], 16)

            def load_res(b):
                sp.dma_start(res[:], x[b]).then_inc(res_loaded, 16)

            def store(b):
                for m in range(KD):
                    sp.wait_ge(out_ready, b * KD + m + 1)
                    sp.dma_start(out[b, :, m, :], res[:, m, :]).then_inc(out_stored, 16)

            sp.dma_start(x_in[:, 0, :], x[0, :, 0, :]).then_inc(x_loaded[0], 16)
            sp.dma_start(raw_w2[:, 0, :], w2[:, 0, :]).then_inc(w2_loaded[0], 16)
            for k in range(1, KD):
                sp.dma_start(x_in[:, k, :], x[0, :, k, :]).then_inc(x_loaded[k], 16)
                sp.dma_start(raw_w2[:, k, :], w2[:, k, :]).then_inc(w2_loaded[k], 16)
            sp.dma_start(raw_narrow[:], narrow[:]).then_inc(narrow_loaded, 16)
            for g, (a, b) in enumerate([(0, REC_FIRST), (REC_FIRST, NH)]):
                sp.dma_start(raw_records[:, a:b, :], records[:, a:b, :]).then_inc(record_loaded[g], 16)
                if g == 0:
                    sp.dma_start(codes_up[:, 0:1, :], q_up[:, 0:1, :]).then_inc(codes_loaded[0], 16)
                    sp.dma_start(codes_down[:, 0:1, :], q_down[:, 0:1, :]).then_inc(codes_loaded[0], 16)
            for g, (a, b) in enumerate(Q_GROUPS):
                if g > 0:
                    sp.dma_start(codes_up[:, a:b, :], q_up[:, a:b, :]).then_inc(codes_loaded[g], 16)
                    sp.dma_start(codes_down[:, a:b, :], q_down[:, a:b, :]).then_inc(codes_loaded[g], 16)

            sp.wait_ge(xm_split, KD)
            load_x(1)
            sp.wait_ge(weight_ready, CHUNKS)
            load_res(0)
            store(0)
            with sp.Fori(1, BLOCKS - 1) as b:
                sp.wait_ge(xm_split, b * KD + KD)
                load_x(b + 1)
                sp.wait_ge(out_stored, b * (16 * KD))
                load_res(b)
                store(b)
            sp.wait_ge(out_stored, (BLOCKS - 1) * (16 * KD))
            load_res(BLOCKS - 1)
            store(BLOCKS - 1)
            sp.wait_ge(out_stored, BLOCKS * 16 * KD)

        @block.scalar
        def _(act):
            def relu_tile(source, bias_col, n, ahead):
                act.wait_ge(product_ready, n + 1)
                if not (isinstance(n, int) and n < FULL_SLOTS):
                    act.wait_ge(act_split, n - FULL_SLOTS + 1)
                act.activation(full[:, ahead % FULL_SLOTS, :], source, ACT.Relu, bias=bias_col).then_inc(relu_done, 1)

            def weight_high(c):
                j = c // 2
                dest = w_up_hi[:, j].rearrange("p k h -> p (k h)") if c % 2 == 0 else w_down_hi[:, j, :]
                act.wait_ge(weight_full, c + 1)
                act.copy(dest, weight[:, c % 2, :]).then_inc(weight_hi, 1)

            act.dma_start(raw_cond[:], cond[:]).then_inc(cond_loaded, 16)
            act.dma_start(raw_w3[:], w3[:]).then_inc(cond_loaded, 16)
            act.dma_start(bias[:], biases[:]).then_inc(bias_loaded, 16)
            act.wait_ge(bias_loaded, 16)
            for m in range(KD):
                act.wait_ge(gate_ready, m + 1)
                act.activation(gate[:, m, :], w2_ps[m][:, 0:BATCH], ACT.Relu, bias=b3[:, m:m + 1]).then_inc(gate_done, 1)
            for k in range(KD):
                act.wait_ge(w2_loaded[k], 16)
                act.copy(w2_hi[:, k, :], raw_w2[:, k, :]).then_inc(w2_cast, 1)
            act.wait_ge(narrow_loaded, 16)
            act.copy(expand_up[:], raw_narrow[:, 0, :]).then_inc(narrow_cast, 1)
            act.copy(narrow_r[:], raw_narrow[:, 1:4, :]).then_inc(narrow_cast, 1)
            for g, (a, b) in enumerate([(0, REC_FIRST), (REC_FIRST, NH)]):
                act.wait_ge(record_loaded[g], 16)
                act.copy(record[:, a:b, :], raw_records[:, a:b, :]).then_inc(record_cast, 1)
            weight_high(0)
            for m in range(KD):
                relu_tile(acc[m][:], b2[:, m:m + 1], m, m)
            weight_high(1)
            weight_high(2)

            def body(b, first, last):
                for j in range(NH):
                    relu_tile(up_ps[j % 2][:], b_up[:, j:j + 1], b * EVACS + (KD + j), j)
                    if first:
                        for c in (2 * j + 3, 2 * j + 4):
                            if c < CHUNKS:
                                weight_high(c)
                if not last:
                    for m in range(KD):
                        relu_tile(w2_ps[m][:], b2[:, m:m + 1], b * EVACS + (KD + NH + m), m)

            body(0, True, False)
            with act.Fori(1, BLOCKS - 1) as b:
                body(b, False, False)
            body(BLOCKS - 1, False, True)

        @block.gpsimd
        def _(pool):
            for k in range(KD):
                pool.wait_ge(w2_cast, k + 1)
                pool.tensor_tensor(w2_lo[:, k, :], raw_w2[:, k, :], w2_hi[:, k, :].bitcast(F32),
                                   ALU.subtract).then_inc(w2_split, 1)

            def split_records(g, a, b):
                pool.wait_ge(record_cast, g + 1)
                dest = record[2 * QUAD:P, a:b, P:REC]
                pool.tensor_tensor(dest, raw_records[2 * QUAD:P, a:b, P:REC], dest.bitcast(F32),
                                   ALU.subtract).then_inc(record_split, 1)

            pool.wait_ge(w2_split, KD)
            split_records(0, 0, REC_FIRST)
            pool.wait_ge(narrow_cast, 2)
            pool.tensor_tensor(scale_down[2 * QUAD:P, :], raw_narrow[2 * QUAD:P, 1, :],
                               scale_down[2 * QUAD:P, :].bitcast(F32), ALU.subtract).then_inc(record_split, 1)
            split_records(1, REC_FIRST, NH)

        @block.vector
        def _(dve):
            def modulate(k, b):
                tile = x_in[:, k, :].rearrange("p (b n) -> p b n", n=SEQ)
                dve.wait_ge(x_loaded[k], b * 16 + 16)
                dve.tensor_reduce(sums[:, k, :], tile, AXIS_X, ALU.add).then_inc(summed, 1)
                dve.wait_ge(summed, b * KD + (k + 1))
                dve.scalar_tensor_tensor(out=tile, in0=tile, scalar=float(SEQ),
                                         in1=sums[:, k, :].unsqueeze(2).to_broadcast([P, PER_BLOCK, SEQ]),
                                         op0=ALU.mult, op1=ALU.add).then_inc(shifted, 1)
                dve.wait_ge(shifted, b * KD + (k + 1))
                if isinstance(b, int) and b == 0:
                    dve.wait_ge(gate_done, KD)
                g = gate[:, k, bass.ds(b * PER_BLOCK, PER_BLOCK)]
                dve.tensor_tensor(tile, tile, g.unsqueeze(2).to_broadcast([P, PER_BLOCK, SEQ]),
                                  ALU.mult).then_inc(modulated, 1)

            def split_xm(k, b):
                s = k % XM_SLOTS
                dve.wait_ge(modulated, b * KD + (k + 1))
                if k >= XM_SLOTS:
                    dve.wait_ge(w2_step_done, b * (KD - XM_SLOTS) + (k - XM_SLOTS + 1))
                dve.tensor_copy(xm_hi[:, s, :], x_in[:, k, :]).then_inc(xm_hi_done, 1)
                dve.wait_ge(xm_hi_done, b * KD + (k + 1))
                dve.tensor_tensor(xm_lo[:, s, :], x_in[:, k, :], xm_hi[:, s, :].bitcast(F32),
                                  ALU.subtract).then_inc(xm_split, 1)

            def split_act(hi, lo, n, slot):
                source = full[:, slot % FULL_SLOTS, :]
                dve.wait_ge(relu_done, n + 1)
                dve.tensor_copy(hi, source).then_inc(act_hi_done, 1)
                dve.wait_ge(act_hi_done, n + 1)
                dve.tensor_tensor(lo, source, hi.bitcast(F32), ALU.subtract).then_inc(act_split, 1)

            def dequantize(c):
                j, whole = c // 2, weight[:, c % 2, :]
                codes = (codes_up, codes_down)[c % 2][:, j, :]
                group = next(g for g, (a, b) in enumerate(Q_GROUPS) if a <= j < b)
                if c % 2 == 0 and j == Q_GROUPS[group][0]:
                    dve.wait_ge(codes_loaded[group], 32)
                dve.wait_ge(scale_ready, c + 1)
                if c >= 2:
                    dve.wait_ge(weight_ready, c - 1)
                dve.scalar_tensor_tensor(out=whole, in0=codes, scalar=-ZERO_POINT, in1=scale_ps[:],
                                         op0=ALU.add, op1=ALU.mult).then_inc(dequant_done, 1)
                dve.wait_ge(dequant_done, c + 1)
                dve.wait_ge(lora_ready, c + 1)
                dve.tensor_tensor(whole, whole, lora_ps[:], ALU.add).then_inc(weight_full, 1)

            def weight_low(c):
                j = c // 2
                pair = ((w_up_hi, w_up_lo) if c % 2 == 0 else (w_down_hi, w_down_lo))
                hi, lo = (w[:, j].rearrange("p k h -> p (k h)") if c % 2 == 0 else w[:, j, :] for w in pair)
                dve.wait_ge(weight_hi, c + 1)
                dve.tensor_tensor(lo, weight[:, c % 2, :], hi.bitcast(F32), ALU.subtract).then_inc(weight_ready, 1)

            def split_narrow():
                dve.wait_ge(narrow_cast, 2)
                for q in (1, 3):
                    rows = slice(q * QUAD, (q + 1) * QUAD)
                    dve.tensor_tensor(narrow_r[rows, 1:3, :], raw_narrow[rows, 2:4, :],
                                      narrow_r[rows, 1:3, :].bitcast(F32), ALU.subtract).then_inc(narrow_split, 1)

            for k in range(KD):
                modulate(k, 0)
                split_xm(k, 0)
            split_narrow()
            dequantize(0)
            for m in range(KD):
                split_act(x1_hi[:, m, :], x1_lo[:, m, :], m, m)
                if m == 0:
                    weight_low(0)
            dequantize(1)
            dequantize(2)
            weight_low(1)

            def body(b, first, last):
                for j in range(NH):
                    s = j % X2_SLOTS
                    if j >= X2_SLOTS:
                        dve.wait_ge(down_done, b * (NH - 1) + (j - X2_SLOTS + 1))
                    split_act(x2_hi[:, s, :], x2_lo[:, s, :], b * EVACS + (KD + j), j)
                    if first:
                        for c in (2 * j + 3, 2 * j + 4):
                            if c < CHUNKS:
                                dequantize(c)
                            if c - 1 < CHUNKS:
                                weight_low(c - 1)
                    if not last:
                        if 4 <= j < 4 + 2 * KD and j % 2 == 0:
                            modulate((j - 4) // 2, b + 1)
                        if NH - 4 <= j < NH - 4 + XM_SLOTS:
                            split_xm(j - (NH - 4), b + 1)
                if not last:
                    for k in range(XM_SLOTS, KD):
                        split_xm(k, b + 1)
                    for m in range(KD):
                        split_act(x1_hi[:, m, :], x1_lo[:, m, :], b * EVACS + (KD + NH + m), m)
                dve.wait_ge(res_loaded, b * 16 + 16)
                for m in range(KD):
                    dve.wait_ge(acc_done, b * KD + (m + 1))
                    dve.scalar_tensor_tensor(out=res[:, m, :], in0=acc[m][:], scalar=b_down[:, m:m + 1],
                                             in1=res[:, m, :], op0=ALU.add, op1=ALU.add).then_inc(out_ready, 1)

            body(0, True, False)
            with dve.Fori(1, BLOCKS - 1) as b:
                body(b, False, False)
            body(BLOCKS - 1, False, True)

        @block.tensor
        def _(pe):
            def three_passes(dest, w_hi, w_lo, a_hi, a_lo, start, stop):
                pe.matmul(dest, w_hi, a_hi, start=start, stop=False)
                pe.matmul(dest, w_hi, a_lo, start=False, stop=False)
                return pe.matmul(dest, w_lo, a_hi, start=False, stop=stop)

            def w2_step(k, b, banks):
                s = k % XM_SLOTS
                pe.wait_ge(xm_split, b * KD + (k + 1))
                for m in range(KD):
                    cols = slice(m * P, (m + 1) * P)
                    mm = three_passes(banks[m][:], w2_hi[:, k, cols], w2_lo[:, k, cols], xm_hi[:, s, :], xm_lo[:, s, :],
                                      k == 0, k == KD - 1)
                    if k == KD - 1:
                        mm.then_inc(product_ready, 1)
                if k < KD - XM_SLOTS:
                    mm.then_inc(w2_step_done, 1)

            def expand(c):
                j = c // 2
                rows, scale_up, wide = (record[:, j, i * P:(i + 1) * P] for i in range(3))
                if c >= 1:
                    pe.wait_ge(dequant_done, c)
                if c % 2 == 0:
                    for k in range(KD):
                        cols = slice(k * P, (k + 1) * P)
                        mm = pe.matmul(scale_ps[:, cols], expand_up[:, cols], scale_up, start=True, stop=True)
                else:
                    mm = pe.matmul(scale_ps[:], rows, scale_down, start=True, stop=True)
                mm.then_inc(scale_ready, 1)
                if c >= 1:
                    pe.wait_ge(weight_full, c)
                if c % 2 == 0:
                    for k in range(KD):
                        cols = slice(k * P, (k + 1) * P)
                        mm = pe.matmul(lora_ps[:, cols], lora_up[:, cols], wide, start=True, stop=True)
                else:
                    mm = pe.matmul(lora_ps[:], wide, lora_down, start=True, stop=True)
                mm.then_inc(lora_ready, 1)

            def up(j, b, first):
                if j == 0:
                    pe.wait_ge(act_split, b * EVACS + KD)
                if j >= 2:
                    pe.wait_ge(relu_done, b * EVACS + (KD + j - 1))
                if first:
                    pe.wait_ge(weight_ready, 2 * j + 1)
                for k in range(KD):
                    mm = three_passes(up_ps[j % 2][:], w_up_hi[:, j, k, :], w_up_lo[:, j, k, :],
                                      x1_hi[:, k, :], x1_lo[:, k, :], k == 0, k == KD - 1)
                mm.then_inc(product_ready, 1)

            def down(j, b, first):
                s = j % X2_SLOTS
                pe.wait_ge(act_split, b * EVACS + (KD + j + 1))
                if first:
                    pe.wait_ge(weight_ready, 2 * j + 2)
                for m in range(KD):
                    if j == 0 and not first:
                        pe.wait_ge(out_ready, b * KD + (m + 1 - KD))
                    cols = slice(m * P, (m + 1) * P)
                    mm = three_passes(acc[m][:], w_down_hi[:, j, cols], w_down_lo[:, j, cols],
                                      x2_hi[:, s, :], x2_lo[:, s, :], j == 0, j == NH - 1)
                    if j == NH - 1:
                        mm.then_inc(acc_done, 1)
                if j < NH - 1:
                    mm.then_inc(down_done, 1)

            def body(b, first, last):
                for j in range(NH):
                    up(j, b, first)
                    if first and 2 * j + 3 < CHUNKS:
                        expand(2 * j + 3)
                    if j >= LAG:
                        down(j - LAG, b, first)
                    if first and 2 * j + 4 < CHUNKS:
                        expand(2 * j + 4)
                if not last:
                    pe.wait_ge(relu_done, b * EVACS + (KD + NH))
                    for k in range(KD):
                        w2_step(k, b + 1, w2_ps)
                for j in range(HELD, NH):
                    down(j, b, first)

            pe.wait_ge(cond_loaded, 32)
            for m in range(KD):
                for k in range(KC):
                    mm = pe.matmul(w2_ps[m][:, 0:BATCH], raw_w3[:, k, m * P:(m + 1) * P], raw_cond[:, k, :],
                                   start=(k == 0), stop=(k == KC - 1))
                mm.then_inc(gate_ready, 1)
            for k in range(KD):
                pe.wait_ge(w2_split, k + 1)
                w2_step(k, 0, acc)
                if k == KD - 2:
                    pe.wait_ge(gate_done, KD)
                    pe.wait_ge(record_split, 2)
                    pe.wait_ge(narrow_split, 2)
                    expand(0)
            expand(1)
            expand(2)
            pe.wait_ge(record_split, 3)
            body(0, True, False)
            with pe.Fori(1, BLOCKS - 1) as b:
                body(b, False, False)
            body(BLOCKS - 1, False, True)


def kernel(**inputs):
    import numpy as np
    import concourse.bacc as bacc
    from concourse.bass_utils import run_bass_kernel_spmd

    a = {k.replace("L0_", ""): np.asarray(v) for k, v in inputs.items()}
    batch, seq, d = a["x"].shape
    hidden = a["ffn_w_up_q"].shape[0]
    kd, nh, nk = d // P, hidden // P, a["cond_W3"].shape[0] // P
    blocks = batch * seq // BANK
    rank = a["ffn_w_up_lora_a"].shape[1]
    group = hidden // a["ffn_w_down_scale"].shape[1]

    def tiles(w):
        return w.reshape(-1, P, w.shape[1]).transpose(1, 0, 2)

    def column(b):
        return b.reshape(-1, P).T

    def by_quadrant(w, quadrants, first):
        out = np.zeros((P, w.shape[1]), np.float32)
        for q in quadrants:
            out[q * QUAD + first:q * QUAD + first + w.shape[0]] = w
        return out

    every, high_low = range(4), (0, 2)
    feature_group = np.arange(hidden) // group
    expander = by_quadrant((np.arange(QUAD)[:, None] == feature_group[None, :]).astype(np.float32), high_low, 0)
    scale_up = by_quadrant(a["ffn_w_up_scale"].T, high_low, 0)
    wide = by_quadrant(a["ffn_w_up_lora_b"], every, 0)
    for q in every:
        wide[q * QUAD + rank:q * QUAD + 2 * rank] = a["ffn_w_down_lora_a"].T
    records = np.stack([w.reshape(P, nh, P) for w in (expander, scale_up, wide)], 2).reshape(P, nh, 3 * P)
    narrow = np.stack([expander[:, :d], by_quadrant(a["ffn_w_down_scale"].T, high_low, 0),
                       by_quadrant(a["ffn_w_up_lora_a"].T, every, 0),
                       by_quadrant(a["ffn_w_down_lora_b"], every, rank)], 1)
    arrays = {
        "x": a["x"].reshape(blocks, BANK, kd, P).transpose(0, 3, 2, 1),
        "cond": tiles(a["cond_1024"].T),
        "w3": tiles(a["cond_W3"]),
        "w2": tiles(a["cond_W2"]),
        "biases": np.concatenate([column(a[n]) for n in ("ffn_b_up", "ffn_b_down", "cond_b2", "cond_b3")], 1),
        "q_up": a["ffn_w_up_q"].reshape(nh, P, kd, P).transpose(3, 0, 2, 1).reshape(P, nh, d),
        "q_down": a["ffn_w_down_q"].reshape(d, nh, P).transpose(2, 1, 0),
        "narrow": narrow,
        "records": records,
    }
    nc = bacc.Bacc("TRN2", target_bir_lowering=False, num_devices=1)
    sent, args = {}, []
    for name, value in arrays.items():
        value = np.ascontiguousarray(value)
        sent[f"in_{name}"] = value
        args.append(nc.dram_tensor(f"in_{name}", value.shape, mybir.dt.from_np(value.dtype), kind="ExternalInput").ap())
    shape = (blocks, P, kd, BANK)
    args.append(nc.dram_tensor("out", shape, F32, kind="ExternalOutput").ap())
    adaln_ffn(nc, *args)
    got = run_bass_kernel_spmd(nc, [sent], core_ids=[0]).results[0]["out"]
    return np.ascontiguousarray(got.reshape(shape).transpose(0, 3, 2, 1)).reshape(batch, seq, d)
```

```python
from contextlib import ExitStack

import concourse.bass as bass
from concourse import mybir

P = 128
QUAD = 32
BANK = 512
PARTS = 3
ALU = mybir.AluOpType
ACT = mybir.ActivationFunctionType
AXIS_X = mybir.AxisListType.X
F32 = mybir.dt.float32
F32R = mybir.dt.float32r
I32 = mybir.dt.int32


def adaln_ffn(nc, x, cond, w3, w2, biases, q_up, q_down, narrow, records, out):
    BLOCKS, _, KD, ROWS = x.shape
    KC, BATCH = cond.shape[1], cond.shape[2]
    D = KD * P
    NH = q_up.shape[1]
    SEQ = 64
    PER_BLOCK = ROWS // SEQ
    ZERO_POINT = 7.5
    X2_SLOTS, XM_SLOTS, FULL_SLOTS = 3, 2, 2
    LAG = 2
    HELD = NH - LAG
    EVACS = NH + KD
    GROUPS = [(0, 2), (2, 4), (4, 8), (8, 12), (12, NH)]
    ONE, PAIR, DOWN = range(3)

    pairs = [(PAIR, t, half) for t in range(2, NH, 2) for half in range(2)]
    downs = [(DOWN, t) for t in range(NH)]
    CHUNKS = [(ONE, 0), (ONE, 1)] + pairs[:2]
    for n in range(NH):
        CHUNKS += downs[n:n + 1] + pairs[n + 2:n + 3]
    UP_NEEDS = [1 + max(e for e, c in enumerate(CHUNKS) if c[0] != DOWN and c[1] == (t if t < 2 else t - t % 2))
                for t in range(NH)]
    DOWN_NEEDS = [1 + CHUNKS.index((DOWN, t)) for t in range(NH)]

    PRODUCTS = []
    for t in range(NH):
        PRODUCTS += [("up", t)] + [("down", t - LAG)] * (t >= LAG)
    AHEAD = 3
    MADE_AFTER = [[e for e in ([AHEAD + i] if i < 1 else [AHEAD + 1, AHEAD + 2] if i == 1 else [AHEAD + 1 + i])
                   if e < len(CHUNKS)] for i in range(len(PRODUCTS))]
    assert ROWS == BANK and BLOCKS >= 3 and KD == 4 and sum(map(len, MADE_AFTER)) == len(CHUNKS) - AHEAD

    SUM_AFTER = [("up", 4 + 2 * k) for k in range(KD)]
    SHIFT_AFTER = [("down", 4 + 2 * k - LAG) for k in range(KD)]
    MODULATE_AFTER = [("up", 5 + 2 * k) for k in range(KD)]
    SPLIT_AFTER = [("up", NH - XM_SLOTS + k) for k in range(XM_SLOTS)]

    def records_needed(e):
        last = CHUNKS[e][1] + (CHUNKS[e][0] == PAIR)
        return next(g for g, (a, b) in enumerate(GROUPS) if a <= last < b) + 1

    with ExitStack() as ctx:
        base = (nc.sbuf_base + 63) // 64 * 64
        size = {}
        place = {}
        at = base
        for name, count in [
            ("w_up_hi", NH * D), ("w_up_lo", NH * D), ("w_down_hi", NH * D), ("w_down_lo", NH * D),
            ("w2_hi", KD * D), ("w2_lo", KD * D), ("x_in", KD * ROWS), ("res", KD * ROWS),
            ("xm_hi", XM_SLOTS * ROWS), ("xm_lo", XM_SLOTS * ROWS), ("x1_hi", KD * ROWS), ("x1_lo", KD * ROWS),
            ("x2_hi", X2_SLOTS * ROWS), ("x2_lo", X2_SLOTS * ROWS), ("full", FULL_SLOTS * ROWS),
            ("gate", KD * BATCH), ("sums", KD * PER_BLOCK), ("biases", biases.shape[1]), ("narrow", 3 * D),
        ]:
            place[name] = at
            at += (4 * count + 31) // 32 * 32
        ctx.enter_context(nc.sbuf_tensor("arena", [P, (at - nc.sbuf_base + 3) // 4 + 8], F32))

        def sb(name, shape, dt, over=None, skip=0):
            return nc.alloc_sbuf_tensor_at(name, shape, dt, offset=place[over or name] + skip)

        w_up_hi = sb("w_up_hi", [P, NH, KD, P], F32R)
        w_up_lo = sb("w_up_lo", [P, NH, KD, P], F32R)
        w_down_hi = sb("w_down_hi", [P, NH, D], F32R)
        w_down_lo = sb("w_down_lo", [P, NH, D], F32R)
        w2_hi = sb("w2_hi", [P, KD, D], F32R)
        w2_lo = sb("w2_lo", [P, KD, D], F32R)
        x_in = sb("x_in", [P, KD, ROWS], F32)
        res = sb("res", [P, KD, ROWS], F32)
        xm_hi = sb("xm_hi", [P, XM_SLOTS, ROWS], F32R)
        xm_lo = sb("xm_lo", [P, XM_SLOTS, ROWS], F32R)
        x1_hi = sb("x1_hi", [P, KD, ROWS], F32R)
        x1_lo = sb("x1_lo", [P, KD, ROWS], F32R)
        x2_hi = sb("x2_hi", [P, X2_SLOTS, ROWS], F32R)
        x2_lo = sb("x2_lo", [P, X2_SLOTS, ROWS], F32R)
        full = sb("full", [P, FULL_SLOTS, ROWS], F32)
        gate = sb("gate", [P, KD, BATCH], F32)
        sums = sb("sums", [P, KD, PER_BLOCK], F32)
        bias = sb("biases", [P, biases.shape[1]], F32)
        b_up, b_down = bias[:, 0:NH], bias[:, NH:NH + KD]
        b2, b3 = bias[:, NH + KD:NH + 2 * KD], bias[:, NH + 2 * KD:NH + 3 * KD]
        narrow_r = sb("narrow", [P, 3, D], F32R)
        lora_up, scale_down, lora_down = narrow_r[:, 0, :], narrow_r[:, 1, :], narrow_r[:, 2, :]
        codes_up = sb("codes_up", [P, NH, D], I32, over="w_up_lo")
        codes_down = sb("codes_down", [P, NH, D], I32, over="w_down_lo")
        REC = 3 * P
        REC_SKIP = 4 * NH * (D - REC)
        raw_narrow = sb("raw_narrow", [P, 4, D], F32, over="w_up_hi")
        raw_records = sb("raw_records", [P, NH, REC], F32, over="w_up_hi", skip=REC_SKIP)
        record = sb("record", [P, NH, REC], F32R, over="w_down_hi", skip=REC_SKIP)
        raw_w2 = sb("raw_w2", [P, KD, D], F32, over="w_down_hi")
        assert 4 * 4 * D <= REC_SKIP
        weight = sb("weight", [P, 2, D], F32, over="res")
        expand_up = sb("expand_up", [P, D], F32R, over="res", skip=2 * 4 * D)
        raw_w3 = sb("raw_w3", [P, KC, D], F32, over="x2_hi")
        raw_cond = sb("raw_cond", [P, KC, BATCH], F32, over="x2_lo")

        acc = [ctx.enter_context(nc.psum_tensor(f"acc{m}", [P, BANK], F32)) for m in range(KD)]
        up_ps = [ctx.enter_context(nc.psum_tensor(f"up_ps{m}", [P, BANK], F32)) for m in range(2)]
        scale_ps = ctx.enter_context(nc.psum_tensor("scale_ps", [P, BANK], F32))
        lora_ps = ctx.enter_context(nc.psum_tensor("lora_ps", [P, BANK], F32))
        w2_ps = [up_ps[0], up_ps[1], scale_ps, lora_ps]

        def sem(name):
            return ctx.enter_context(nc.semaphore(name))

        cond_loaded, bias_loaded, narrow_loaded = sem("cond_loaded"), sem("bias_loaded"), sem("narrow_loaded")
        w2_loaded = [sem(f"w2_loaded{k}") for k in range(KD)]
        record_loaded = [sem(f"record_loaded{g}") for g in range(len(GROUPS))]
        codes_loaded = [sem(f"codes_loaded{g}") for g in range(len(GROUPS))]
        x_loaded = [sem(f"x_loaded{k}") for k in range(KD)]
        res_loaded, out_stored = sem("res_loaded"), sem("out_stored")
        w2_cast, w2_split = sem("w2_cast"), sem("w2_split")
        narrow_cast, lora_up_split, lora_down_split, scale_down_split = (
            sem("narrow_cast"), sem("lora_up_split"), sem("lora_down_split"), sem("scale_down_split"))
        record_cast, record_split = sem("record_cast"), sem("record_split")
        gate_ready, gate_done = sem("gate_ready"), sem("gate_done")
        table_loaded = sem("table_loaded")
        scale_ready, lora_ready = sem("scale_ready"), sem("lora_ready")
        dequant_done, weight_full, weight_hi, weight_ready = (
            sem("dequant_done"), sem("weight_full"), sem("weight_hi"), sem("weight_ready"))
        summed, shifted, modulated = sem("summed"), sem("shifted"), sem("modulated")
        xm_hi_done, xm_split = sem("xm_hi_done"), sem("xm_split")
        w2_step_done = sem("w2_step_done")
        product_ready, relu_done, act_hi_done, act_split = (
            sem("product_ready"), sem("relu_done"), sem("act_hi_done"), sem("act_split"))
        down_done = sem("down_done")
        acc_done, out_ready = sem("acc_done"), sem("out_ready")

        codes_up4 = codes_up[:].rearrange("p t (k h) -> p t k h", h=P)

        def part_of(e, up_weights, down_weights):
            form, t = CHUNKS[e][:2]
            if form == DOWN:
                return down_weights[:, t, :]
            if form == ONE:
                return up_weights[:, t].rearrange("p k h -> p (k h)")
            half = CHUNKS[e][2]
            return up_weights[:, t:t + 2, 2 * half:2 * half + 2, :].rearrange("p t k h -> p t (k h)")

        def like(e, bank):
            return bank[:].rearrange("p (t c) -> p t c", t=2) if CHUNKS[e][0] == PAIR else bank[:]

        def scratch(e):
            return like(e, weight[:, e % 2, :])

        block = ctx.enter_context(nc.Block())

        @block.sync
        def _(sp):
            def load_x(b):
                for k in range(KD):
                    sp.dma_start(x_in[:, k, :], x[b, :, k, :]).then_inc(x_loaded[k], 16)

            def load_res(b):
                sp.dma_start(res[:], x[b]).then_inc(res_loaded, 16)

            def store(b):
                for m in range(KD):
                    sp.wait_ge(out_ready, b * KD + m + 1)
                    sp.dma_start(out[b, :, m, :], res[:, m, :]).then_inc(out_stored, 16)

            def load_group(g):
                a, b = GROUPS[g]
                sp.dma_start(raw_records[:, a:b, :], records[:, a:b, :]).then_inc(record_loaded[g], 16)

            def load_codes(g):
                a, b = GROUPS[g]
                sp.dma_start(codes_up[:, a:b, :], q_up[:, a:b, :]).then_inc(codes_loaded[g], 16)
                sp.dma_start(codes_down[:, a:b, :], q_down[:, a:b, :]).then_inc(codes_loaded[g], 16)

            for k in range(KD):
                sp.dma_start(x_in[:, k, :], x[0, :, k, :]).then_inc(x_loaded[k], 16)
                if k == 0:
                    sp.dma_start(raw_w3[:], w3[:]).then_inc(cond_loaded, 16)
                if k < KD - 1:
                    sp.dma_start(raw_w2[:, k, :], w2[:, k, :]).then_inc(w2_loaded[k], 16)
            sp.dma_start(raw_narrow[:], narrow[:]).then_inc(narrow_loaded, 16)
            load_group(0)
            sp.dma_start(raw_w2[:, KD - 1, :], w2[:, KD - 1, :]).then_inc(w2_loaded[KD - 1], 16)
            load_codes(0)
            for g in range(1, len(GROUPS)):
                load_group(g)
                load_codes(g)

            sp.wait_ge(xm_split, KD)
            load_x(1)
            sp.wait_ge(weight_ready, len(CHUNKS))
            load_res(0)
            store(0)
            with sp.Fori(1, BLOCKS - 1) as b:
                sp.wait_ge(xm_split, b * KD + KD)
                load_x(b + 1)
                sp.wait_ge(out_stored, b * (16 * KD))
                load_res(b)
                store(b)
            sp.wait_ge(out_stored, (BLOCKS - 1) * (16 * KD))
            load_res(BLOCKS - 1)
            store(BLOCKS - 1)
            sp.wait_ge(out_stored, BLOCKS * 16 * KD)

        @block.scalar
        def _(act):
            def relu_tile(source, bias_col, n, slot, hi):
                whole = full[:, slot % FULL_SLOTS, :]
                act.wait_ge(product_ready, n + 1)
                if not (isinstance(n, int) and n < FULL_SLOTS):
                    act.wait_ge(act_split, n - FULL_SLOTS + 1)
                act.activation(whole, source, ACT.Relu, bias=bias_col).then_inc(relu_done, 1)
                act.wait_ge(relu_done, n + 1)
                act.copy(hi, whole).then_inc(act_hi_done, 1)

            def weight_high(e):
                act.wait_ge(weight_full, e + 1)
                act.copy(part_of(e, w_up_hi, w_down_hi), scratch(e)).then_inc(weight_hi, 1)

            def cast_records(g):
                a, b = GROUPS[g]
                act.wait_ge(record_loaded[g], 16)
                act.copy(record[:, a:b, :], raw_records[:, a:b, :]).then_inc(record_cast, 1)

            act.dma_start(raw_cond[:], cond[:]).then_inc(cond_loaded, 16)
            act.dma_start(bias[:], biases[:]).then_inc(bias_loaded, 16)
            act.wait_ge(bias_loaded, 16)
            act.activation(sums[:, 0, 0:KD], b3, ACT.Relu).then_inc(table_loaded, 1)
            act.wait_ge(gate_ready, 1)
            act.activation(gate[:, 0, :], w2_ps[0][:, 0:BATCH], ACT.Relu, bias=b3[:, 0:1]).then_inc(gate_done, 1)
            for k in range(KD):
                if k > 0:
                    act.wait_ge(gate_ready, k + 1)
                    act.activation(gate[:, k, :], w2_ps[k][:, 0:BATCH], ACT.Relu, bias=b3[:, k:k + 1]).then_inc(gate_done, 1)
                if k < KD - 1:
                    act.wait_ge(w2_loaded[k], 16)
                    act.copy(w2_hi[:, k, :], raw_w2[:, k, :]).then_inc(w2_cast, 1)
            act.wait_ge(narrow_loaded, 16)
            act.copy(expand_up[:], raw_narrow[:, 0, :]).then_inc(narrow_cast, 1)
            act.copy(lora_up, raw_narrow[:, 1, :]).then_inc(narrow_cast, 1)
            cast_records(0)
            act.wait_ge(w2_loaded[KD - 1], 16)
            act.copy(w2_hi[:, KD - 1, :], raw_w2[:, KD - 1, :]).then_inc(w2_cast, 1)
            act.copy(narrow_r[:, 1:3, :], raw_narrow[:, 2:4, :]).then_inc(narrow_cast, 1)
            cast_records(1)
            weight_high(0)
            for m in range(KD):
                relu_tile(acc[m][:], b2[:, m:m + 1], m, m, x1_hi[:, m, :])
            cast_records(2)
            weight_high(1)
            weight_high(2)

            def body(b, first, last):
                for i, (kind, j) in enumerate(PRODUCTS):
                    if kind == "up":
                        if j >= X2_SLOTS:
                            act.wait_ge(down_done, b * (NH - 1) + (j - X2_SLOTS + 1))
                        relu_tile(up_ps[j % 2][:], b_up[:, j:j + 1], b * EVACS + (KD + j), j, x2_hi[:, j % X2_SLOTS, :])
                    if first:
                        for e in MADE_AFTER[i]:
                            weight_high(e)
                        if i in (2, 4):
                            cast_records(2 + i // 2)
                if not last:
                    for m in range(KD):
                        relu_tile(w2_ps[m][:], b2[:, m:m + 1], b * EVACS + (KD + NH + m), m, x1_hi[:, m, :])

            body(0, True, False)
            with act.Fori(1, BLOCKS - 1) as b:
                body(b, False, False)
            body(BLOCKS - 1, False, True)

        @block.gpsimd
        def _(pool):
            def low_of_w2(k):
                pool.wait_ge(w2_cast, k + 1)
                pool.tensor_tensor(w2_lo[:, k, :], raw_w2[:, k, :], w2_hi[:, k, :].bitcast(F32),
                                   ALU.subtract).then_inc(w2_split, 1)

            def low_of_records(g):
                a, b = GROUPS[g]
                dest = record[2 * QUAD:P, a:b, P:REC]
                pool.wait_ge(record_cast, g + 1)
                pool.tensor_tensor(dest, raw_records[2 * QUAD:P, a:b, P:REC], dest.bitcast(F32),
                                   ALU.subtract).then_inc(record_split, 1)

            for k in range(KD - 1):
                low_of_w2(k)
            pool.wait_ge(w2_split, KD - 1)
            low_of_records(0)
            pool.wait_ge(record_split, 1)
            low_of_w2(KD - 1)
            pool.wait_ge(w2_split, KD)
            pool.wait_ge(narrow_cast, 3)
            pool.tensor_tensor(scale_down[2 * QUAD:P, :], raw_narrow[2 * QUAD:P, 2, :],
                               scale_down[2 * QUAD:P, :].bitcast(F32), ALU.subtract).then_inc(scale_down_split, 1)
            pool.wait_ge(scale_down_split, 1)
            for n, q in enumerate((1, 3)):
                rows = slice(q * QUAD, (q + 1) * QUAD)
                pool.tensor_tensor(lora_down[rows, :], raw_narrow[rows, 3, :], lora_down[rows, :].bitcast(F32),
                                   ALU.subtract).then_inc(lora_down_split, 1)
                pool.wait_ge(lora_down_split, n + 1)
            for g in range(1, len(GROUPS)):
                low_of_records(g)

        @block.vector
        def _(dve):
            def batches(k):
                return x_in[:, k, :].rearrange("p (b n) -> p b n", n=SEQ)

            def sum_up(k, b):
                dve.wait_ge(x_loaded[k], b * 16 + 16)
                dve.tensor_reduce(sums[:, k, :], batches(k), AXIS_X, ALU.add).then_inc(summed, 1)

            def shift(k, b):
                dve.wait_ge(summed, b * KD + (k + 1))
                dve.scalar_tensor_tensor(out=batches(k), in0=batches(k), scalar=float(SEQ),
                                         in1=sums[:, k, :].unsqueeze(2).to_broadcast([P, PER_BLOCK, SEQ]),
                                         op0=ALU.mult, op1=ALU.add).then_inc(shifted, 1)

            def modulate(k, b):
                dve.wait_ge(shifted, b * KD + (k + 1))
                if isinstance(b, int) and b == 0:
                    dve.wait_ge(gate_done, k + 1)
                g = gate[:, k, bass.ds(b * PER_BLOCK, PER_BLOCK)]
                dve.tensor_tensor(batches(k), batches(k), g.unsqueeze(2).to_broadcast([P, PER_BLOCK, SEQ]),
                                  ALU.mult).then_inc(modulated, 1)

            def split_xm(k, b):
                s = k % XM_SLOTS
                dve.wait_ge(modulated, b * KD + (k + 1))
                if k >= XM_SLOTS:
                    dve.wait_ge(w2_step_done, b * (KD - XM_SLOTS) + (k - XM_SLOTS + 1))
                dve.tensor_copy(xm_hi[:, s, :], x_in[:, k, :]).then_inc(xm_hi_done, 1)
                dve.wait_ge(xm_hi_done, b * KD + (k + 1))
                dve.tensor_tensor(xm_lo[:, s, :], x_in[:, k, :], xm_hi[:, s, :].bitcast(F32),
                                  ALU.subtract).then_inc(xm_split, 1)

            def low_of_act(hi, lo, n, slot):
                dve.wait_ge(act_hi_done, n + 1)
                dve.tensor_tensor(lo, full[:, slot % FULL_SLOTS, :], hi.bitcast(F32), ALU.subtract).then_inc(act_split, 1)

            def dequantize(e):
                group = records_needed(e) - 1
                if e == 0 or group != records_needed(e - 1) - 1:
                    dve.wait_ge(codes_loaded[group], 32)
                dve.wait_ge(scale_ready, e + 1)
                if e >= 2:
                    dve.wait_ge(weight_ready, e - 1)
                dve.scalar_tensor_tensor(out=scratch(e), in0=part_of(e, codes_up4, codes_down), scalar=-ZERO_POINT,
                                         in1=like(e, scale_ps), op0=ALU.add, op1=ALU.mult).then_inc(dequant_done, 1)
                dve.wait_ge(dequant_done, e + 1)
                dve.wait_ge(lora_ready, e + 1)
                dve.tensor_tensor(scratch(e), scratch(e), like(e, lora_ps), ALU.add).then_inc(weight_full, 1)

            def weight_low(e):
                dve.wait_ge(weight_hi, e + 1)
                dve.tensor_tensor(part_of(e, w_up_lo, w_down_lo), scratch(e),
                                  part_of(e, w_up_hi, w_down_hi).bitcast(F32), ALU.subtract).then_inc(weight_ready, 1)

            dve.wait_ge(table_loaded, 1)
            for k in range(KD):
                if k == KD - 1:
                    dve.wait_ge(narrow_cast, 2)
                    for q in (1, 3):
                        rows = slice(q * QUAD, (q + 1) * QUAD)
                        dve.tensor_tensor(lora_up[rows, :], raw_narrow[rows, 1, :], lora_up[rows, :].bitcast(F32),
                                          ALU.subtract).then_inc(lora_up_split, 1)
                sum_up(k, 0)
                shift(k, 0)
                modulate(k, 0)
                split_xm(k, 0)
            dequantize(0)
            for m in range(KD):
                low_of_act(x1_hi[:, m, :], x1_lo[:, m, :], m, m)
                if m == 0:
                    weight_low(0)
                if m == 1:
                    dequantize(1)
            weight_low(1)
            dequantize(2)
            weight_low(2)

            def body(b, first, last):
                for i, (kind, j) in enumerate(PRODUCTS):
                    made = MADE_AFTER[i] if first else []
                    for e in made:
                        dequantize(e)
                        if e != made[-1]:
                            weight_low(e)
                    if kind == "up":
                        s = j % X2_SLOTS
                        low_of_act(x2_hi[:, s, :], x2_lo[:, s, :], b * EVACS + (KD + j), j)
                    for e in made[-1:]:
                        weight_low(e)
                    if not last and (kind, j) in SUM_AFTER:
                        sum_up(SUM_AFTER.index((kind, j)), b + 1)
                    if not last and (kind, j) in SHIFT_AFTER:
                        shift(SHIFT_AFTER.index((kind, j)), b + 1)
                    if not last and (kind, j) in MODULATE_AFTER:
                        modulate(MODULATE_AFTER.index((kind, j)), b + 1)
                    if not last and (kind, j) in SPLIT_AFTER:
                        split_xm(SPLIT_AFTER.index((kind, j)), b + 1)
                if not last:
                    for k in range(XM_SLOTS, KD):
                        split_xm(k, b + 1)
                    for m in range(KD):
                        low_of_act(x1_hi[:, m, :], x1_lo[:, m, :], b * EVACS + (KD + NH + m), m)
                dve.wait_ge(res_loaded, b * 16 + 16)
                for m in range(KD):
                    dve.wait_ge(acc_done, b * KD + (m + 1))
                    dve.scalar_tensor_tensor(out=res[:, m, :], in0=acc[m][:], scalar=b_down[:, m:m + 1],
                                             in1=res[:, m, :], op0=ALU.add, op1=ALU.add).then_inc(out_ready, 1)

            body(0, True, False)
            with dve.Fori(1, BLOCKS - 1) as b:
                body(b, False, False)
            body(BLOCKS - 1, False, True)

        @block.tensor
        def _(pe):
            def three_passes(dest, w_hi, w_lo, a_hi, a_lo, start, stop):
                pe.matmul(dest, w_hi, a_hi, start=start, stop=False)
                pe.matmul(dest, w_hi, a_lo, start=False, stop=False)
                return pe.matmul(dest, w_lo, a_hi, start=False, stop=stop)

            def w2_step(k, b, banks):
                s = k % XM_SLOTS
                pe.wait_ge(xm_split, b * KD + (k + 1))
                for m in range(KD):
                    cols = slice(m * P, (m + 1) * P)
                    mm = three_passes(banks[m][:], w2_hi[:, k, cols], w2_lo[:, k, cols], xm_hi[:, s, :], xm_lo[:, s, :],
                                      k == 0, k == KD - 1)
                    if k == KD - 1:
                        mm.then_inc(product_ready, 1)
                if k < KD - XM_SLOTS:
                    mm.then_inc(w2_step_done, 1)

            def expand(e):
                form, t = CHUNKS[e][:2]
                if e == 0 or records_needed(e) > records_needed(e - 1):
                    pe.wait_ge(record_split, records_needed(e))
                if CHUNKS[e] == (DOWN, 0):
                    pe.wait_ge(scale_down_split, 1)
                    pe.wait_ge(lora_down_split, 2)
                count = 1 + (form == PAIR)
                rows = record[:, t, 0:P]
                scale_up, wide = (record[:, t:t + count, i * P:(i + 1) * P] for i in (1, 2))
                for bank, still, moving, still_down, moving_down, freed, made in (
                        (scale_ps, expand_up, scale_up, rows, scale_down, dequant_done, scale_ready),
                        (lora_ps, lora_up, wide, record[:, t, 2 * P:3 * P], lora_down, weight_full, lora_ready)):
                    if e >= 1:
                        pe.wait_ge(freed, e)
                    if form == DOWN:
                        mm = pe.matmul(bank[:], still_down, moving_down, start=True, stop=True)
                    else:
                        ks = range(KD) if form == ONE else range(2 * CHUNKS[e][2], 2 * CHUNKS[e][2] + 2)
                        dest = bank[:].rearrange("p (t k h) -> p t k h", t=count, h=P)
                        for n, k in enumerate(ks):
                            mm = pe.matmul(dest[:, :, n, :], still[:, k * P:(k + 1) * P], moving, start=True, stop=True)
                    mm.then_inc(made, 1)

            def up(j, b, first):
                if j == 0:
                    pe.wait_ge(act_split, b * EVACS + KD)
                if j >= 2:
                    pe.wait_ge(relu_done, b * EVACS + (KD + j - 1))
                if first:
                    pe.wait_ge(weight_ready, UP_NEEDS[j])
                for k in range(KD):
                    mm = three_passes(up_ps[j % 2][:], w_up_hi[:, j, k, :], w_up_lo[:, j, k, :],
                                      x1_hi[:, k, :], x1_lo[:, k, :], k == 0, k == KD - 1)
                mm.then_inc(product_ready, 1)

            def down(j, b, first):
                s = j % X2_SLOTS
                pe.wait_ge(act_split, b * EVACS + (KD + j + 1))
                if first:
                    pe.wait_ge(weight_ready, DOWN_NEEDS[j])
                for m in range(KD):
                    if j == 0 and not first:
                        pe.wait_ge(out_ready, b * KD + (m + 1 - KD))
                    cols = slice(m * P, (m + 1) * P)
                    mm = three_passes(acc[m][:], w_down_hi[:, j, cols], w_down_lo[:, j, cols],
                                      x2_hi[:, s, :], x2_lo[:, s, :], j == 0, j == NH - 1)
                    if j == NH - 1:
                        mm.then_inc(acc_done, 1)
                if j < NH - 1:
                    mm.then_inc(down_done, 1)

            def body(b, first, last):
                for i, (kind, j) in enumerate(PRODUCTS):
                    (up if kind == "up" else down)(j, b, first)
                    for e in MADE_AFTER[i] if first else []:
                        expand(e)
                if not last:
                    pe.wait_ge(relu_done, b * EVACS + (KD + NH))
                    for k in range(KD):
                        w2_step(k, b + 1, w2_ps)
                for j in range(HELD, NH):
                    down(j, b, first)

            pe.wait_ge(cond_loaded, 32)
            for m in range(KD):
                for k in range(KC):
                    mm = pe.matmul(w2_ps[m][:, 0:BATCH], raw_w3[:, k, m * P:(m + 1) * P], raw_cond[:, k, :],
                                   start=(k == 0), stop=(k == KC - 1))
                mm.then_inc(gate_ready, 1)
            for k in range(KD):
                pe.wait_ge(w2_split, k + 1)
                w2_step(k, 0, acc)
                if k == KD - 2:
                    pe.wait_ge(gate_done, KD)
                    pe.wait_ge(lora_up_split, 2)
                    expand(0)
            expand(1)
            expand(2)
            body(0, True, False)
            with pe.Fori(1, BLOCKS - 1) as b:
                body(b, False, False)
            body(BLOCKS - 1, False, True)


def kernel(**inputs):
    import numpy as np
    import concourse.bacc as bacc
    from concourse.bass_utils import run_bass_kernel_spmd

    a = {k.replace("L0_", ""): np.asarray(v) for k, v in inputs.items()}
    batch, seq, d = a["x"].shape
    hidden = a["ffn_w_up_q"].shape[0]
    kd, nh, nk = d // P, hidden // P, a["cond_W3"].shape[0] // P
    blocks = batch * seq // BANK
    rank = a["ffn_w_up_lora_a"].shape[1]
    group = hidden // a["ffn_w_down_scale"].shape[1]

    def tiles(w):
        return w.reshape(-1, P, w.shape[1]).transpose(1, 0, 2)

    def column(b):
        return b.reshape(-1, P).T

    def by_quadrant(w, quadrants, first):
        out = np.zeros((P, w.shape[1]), np.float32)
        for q in quadrants:
            out[q * QUAD + first:q * QUAD + first + w.shape[0]] = w
        return out

    every, high_low = range(4), (0, 2)
    feature_group = np.arange(hidden) // group
    expander = by_quadrant((np.arange(QUAD)[:, None] == feature_group[None, :]).astype(np.float32), high_low, 0)
    scale_up = by_quadrant(a["ffn_w_up_scale"].T, high_low, 0)
    wide = by_quadrant(a["ffn_w_up_lora_b"], every, 0)
    for q in every:
        wide[q * QUAD + rank:q * QUAD + 2 * rank] = a["ffn_w_down_lora_a"].T
    records = np.stack([w.reshape(P, nh, P) for w in (expander, scale_up, wide)], 2).reshape(P, nh, 3 * P)
    narrow = np.stack([expander[:, :d], by_quadrant(a["ffn_w_up_lora_a"].T, every, 0),
                       by_quadrant(a["ffn_w_down_scale"].T, high_low, 0),
                       by_quadrant(a["ffn_w_down_lora_b"], every, rank)], 1)
    arrays = {
        "x": a["x"].reshape(blocks, BANK, kd, P).transpose(0, 3, 2, 1),
        "cond": tiles(a["cond_1024"].T),
        "w3": tiles(a["cond_W3"]),
        "w2": tiles(a["cond_W2"]),
        "biases": np.concatenate([column(a[n]) for n in ("ffn_b_up", "ffn_b_down", "cond_b2", "cond_b3")], 1),
        "q_up": a["ffn_w_up_q"].reshape(nh, P, kd, P).transpose(3, 0, 2, 1).reshape(P, nh, d),
        "q_down": a["ffn_w_down_q"].reshape(d, nh, P).transpose(2, 1, 0),
        "narrow": narrow,
        "records": records,
    }
    nc = bacc.Bacc("TRN2", target_bir_lowering=False, num_devices=1)
    sent, args = {}, []
    for name, value in arrays.items():
        value = np.ascontiguousarray(value)
        sent[f"in_{name}"] = value
        args.append(nc.dram_tensor(f"in_{name}", value.shape, mybir.dt.from_np(value.dtype), kind="ExternalInput").ap())
    shape = (blocks, P, kd, BANK)
    args.append(nc.dram_tensor("out", shape, F32, kind="ExternalOutput").ap())
    adaln_ffn(nc, *args)
    got = run_bass_kernel_spmd(nc, [sent], core_ids=[0]).results[0]["out"]
    return np.ascontiguousarray(got.reshape(shape).transpose(0, 3, 2, 1)).reshape(batch, seq, d)
```
